# Optimizing a Trainium2 kernel written in Bass

```python
import numpy as np
import jax
import jax.numpy as jnp

def _softmax(x, axis=-1):
    return jax.nn.softmax(x, axis=axis)

def _gelu(x):
    return jax.nn.gelu(x, approximate=True)

def _silu(x):
    return jax.nn.silu(x)

def _sigmoid(x):
    return jax.nn.sigmoid(x)

def _layernorm(x, axis=-1, eps=1e-05):
    m = jnp.mean(x, axis=axis, keepdims=True)
    v = jnp.var(x, axis=axis, keepdims=True)
    return (x - m) / jnp.sqrt(v + eps)

def _scatter_add(tgt, idx, src, axis=0):
    return tgt.at[idx].add(src)

def _segment_sum(src, seg, n):
    return jax.ops.segment_sum(src, seg, n)
kernel_name = 'mk_prb_d1_jaxref_r4_d07222'

def setup_inputs(seed: int=0):
    np.random.seed(seed)
    _w = jnp.asarray

    def _L0_attn_setup():
        import jax, jax.numpy as jnp
        import numpy as np
        import math
        D_MODEL, N_HEADS, D_K, D_C, D_HR = (256, 8, 128, 32, 32)
        B, S = (4, 512)
        key = jax.random.key(seed)
        ks = jax.random.split(key, 17)

        def lin(k, fan_in, fan_out):
            lim = 1.0 / math.sqrt(fan_in)
            kw, kb = jax.random.split(k)
            W = jax.random.uniform(kw, (fan_in, fan_out), jnp.float32, -lim, lim)
            b = jax.random.uniform(kb, (fan_out,), jnp.float32, -lim, lim)
            return (W, b)
        W_DQ, b_DQ = lin(ks[0], D_MODEL, D_C)
        W_UQ, b_UQ = lin(ks[1], D_C, N_HEADS * D_K)
        W_DKV, b_DKV = lin(ks[2], D_MODEL, D_C)
        W_UK, b_UK = lin(ks[3], D_C, N_HEADS * D_K)
        W_UV, b_UV = lin(ks[4], D_C, N_HEADS * D_K)
        W_QR, b_QR = lin(ks[5], D_C, N_HEADS * D_HR)
        W_KR, b_KR = lin(ks[6], D_MODEL, D_HR)
        W_O, b_O = lin(ks[7], N_HEADS * D_K, D_MODEL)
        h_t = jax.random.normal(ks[8], (B, S, D_MODEL), jnp.float32)
        return {'h_t': h_t, 'W_DQ': W_DQ, 'b_DQ': b_DQ, 'W_UQ': W_UQ, 'b_UQ': b_UQ, 'W_DKV': W_DKV, 'b_DKV': b_DKV, 'W_UK': W_UK, 'b_UK': b_UK, 'W_UV': W_UV, 'b_UV': b_UV, 'W_QR': W_QR, 'b_QR': b_QR, 'W_KR': W_KR, 'b_KR': b_KR, 'W_O': W_O, 'b_O': b_O}
    _L0_attn_in = _L0_attn_setup()

    def _L0_ffn_setup():
        import jax, jax.numpy as jnp
        import numpy as np
        B, N, C, H, REG = (1, 2309, 256, 16, 5)
        D = C // H
        key = jax.random.key(seed)
        k0, k1, k2, k3 = jax.random.split(key, 4)
        x = jax.random.normal(k0, (B, N, C), dtype=jnp.float32)
        g_info = jax.random.normal(k1, (12, 2, C), dtype=jnp.float32)
        W_qkv = jax.random.normal(k2, (C, 3 * C), dtype=jnp.float32) * 0.02
        W_proj = jax.random.normal(k3, (C, C), dtype=jnp.float32) * 0.02
        b_proj = jnp.zeros((C,), dtype=jnp.float32)
        return {'x': x, 'g_info': g_info, 'W_qkv': W_qkv, 'W_proj': W_proj, 'b_proj': b_proj}
    _L0_ffn_in = _L0_ffn_setup()
    _d = {'L0_attn_h_t': _L0_attn_in['h_t'], 'L0_attn_W_DQ': _L0_attn_in['W_DQ'], 'L0_attn_b_DQ': _L0_attn_in['b_DQ'], 'L0_attn_W_UQ': _L0_attn_in['W_UQ'], 'L0_attn_b_UQ': _L0_attn_in['b_UQ'], 'L0_attn_W_DKV': _L0_attn_in['W_DKV'], 'L0_attn_b_DKV': _L0_attn_in['b_DKV'], 'L0_attn_W_UK': _L0_attn_in['W_UK'], 'L0_attn_b_UK': _L0_attn_in['b_UK'], 'L0_attn_W_UV': _L0_attn_in['W_UV'], 'L0_attn_b_UV': _L0_attn_in['b_UV'], 'L0_attn_W_QR': _L0_attn_in['W_QR'], 'L0_attn_b_QR': _L0_attn_in['b_QR'], 'L0_attn_W_KR': _L0_attn_in['W_KR'], 'L0_attn_b_KR': _L0_attn_in['b_KR'], 'L0_attn_W_O': _L0_attn_in['W_O'], 'L0_attn_b_O': _L0_attn_in['b_O'], 'L0_ffn_g_info': _L0_ffn_in['g_info'], 'L0_ffn_W_qkv': _L0_ffn_in['W_qkv'], 'L0_ffn_W_proj': _L0_ffn_in['W_proj'], 'L0_ffn_b_proj': _L0_ffn_in['b_proj']}
    _x0 = _d['L0_attn_h_t']
    _d['L0_attn_h_t'] = jax.random.normal(jax.random.fold_in(jax.random.key(seed), 1), (8, 1024, 256), dtype=_x0.dtype)
    del _x0
    return _d

def reference(L0_attn_h_t, L0_attn_W_DQ, L0_attn_b_DQ, L0_attn_W_UQ, L0_attn_b_UQ, L0_attn_W_DKV, L0_attn_b_DKV, L0_attn_W_UK, L0_attn_b_UK, L0_attn_W_UV, L0_attn_b_UV, L0_attn_W_QR, L0_attn_b_QR, L0_attn_W_KR, L0_attn_b_KR, L0_attn_W_O, L0_attn_b_O, L0_ffn_g_info, L0_ffn_W_qkv, L0_ffn_W_proj, L0_ffn_b_proj):

    def _L0_attn_ref(h_t, W_DQ, b_DQ, W_UQ, b_UQ, W_DKV, b_DKV, W_UK, b_UK, W_UV, b_UV, W_QR, b_QR, W_KR, b_KR, W_O, b_O):
        import jax, jax.numpy as jnp
        import numpy as np
        import math
        D_MODEL, N_HEADS, D_K, D_C, D_HR = (256, 8, 128, 32, 32)
        B, S = (4, 512)
        b, s, _ = h_t.shape
        c_q = h_t @ W_DQ + b_DQ
        c_kv = h_t @ W_DKV + b_DKV
        q_c = (c_q @ W_UQ + b_UQ).reshape(b, s, N_HEADS, D_K).transpose(0, 2, 1, 3)
        k_c = (c_kv @ W_UK + b_UK).reshape(b, s, N_HEADS, D_K).transpose(0, 2, 1, 3)
        v_c = (c_kv @ W_UV + b_UV).reshape(b, s, N_HEADS, D_K).transpose(0, 2, 1, 3)
        q_r = (c_q @ W_QR + b_QR).reshape(b, s, N_HEADS, D_HR).transpose(0, 2, 1, 3)
        k_r = (h_t @ W_KR + b_KR)[:, None, :, :]
        k_r = jnp.broadcast_to(k_r, (b, N_HEADS, s, D_HR))
        q = jnp.concatenate([q_c, q_r], axis=-1)
        k = jnp.concatenate([k_c, k_r], axis=-1)
        scale = 1.0 / math.sqrt(D_K + D_HR)
        scores = jnp.einsum('bhsd,bhtd->bhst', q, k) * scale
        attn = jax.nn.softmax(scores, axis=-1)
        o = jnp.einsum('bhst,bhtd->bhsd', attn, v_c)
        o = o.transpose(0, 2, 1, 3).reshape(b, s, N_HEADS * D_K)
        return o @ W_O + b_O

    def _L0_ffn_ref(x, g_info, W_qkv, W_proj, b_proj):
        import jax, jax.numpy as jnp
        import numpy as np
        B, N, C, H, REG = (1, 2309, 256, 16, 5)
        D = C // H
        Bx, Nx, Cx = x.shape
        scale = D ** (-0.5)
        qkv = (x @ W_qkv).reshape(Bx, Nx, 3, H, D)
        q, k, v = (qkv[:, :, 0], qkv[:, :, 1], qkv[:, :, 2])
        g_layer = g_info[0].reshape(-1, H, D)
        q_g = g_layer[0]
        q_pure = q[:, REG:]
        q_n = q_pure / jnp.linalg.norm(q_pure, axis=-1, keepdims=True)
        qg_n = q_g / jnp.linalg.norm(q_g, axis=-1, keepdims=True)
        sim = (qg_n[None, None] * q_n).sum(-1).mean(-1)
        sim = (sim - sim.min()) / (sim.max() - sim.min())
        pos = sim > 0.9
        logits = jnp.einsum('bqhd,bkhd->bhqk', q * scale, k)

        def masked_attn(tok_mask):
            key_mask = jnp.concatenate([jnp.ones((Bx, REG), bool), tok_mask], axis=1)
            l = jnp.where(key_mask[:, None, None, :], logits, -jnp.inf)
            a = jax.nn.softmax(l, axis=-1)
            return jnp.einsum('bhqk,bkhd->bqhd', a, v)
        x_pos = masked_attn(pos)
        x_neg = masked_attn(~pos)
        reg_out = (x_pos[:, :REG] + x_neg[:, :REG]) * 0.5
        tok_out = jnp.where(pos[:, :, None, None], x_pos[:, REG:], x_neg[:, REG:])
        out = jnp.concatenate([reg_out, tok_out], axis=1).reshape(Bx, Nx, Cx)
        return out @ W_proj + b_proj
    x = L0_attn_h_t
    xn = _layernorm(x, axis=-1)
    x = x + _L0_attn_ref(xn, L0_attn_W_DQ, L0_attn_b_DQ, L0_attn_W_UQ, L0_attn_b_UQ, L0_attn_W_DKV, L0_attn_b_DKV, L0_attn_W_UK, L0_attn_b_UK, L0_attn_W_UV, L0_attn_b_UV, L0_attn_W_QR, L0_attn_b_QR, L0_attn_W_KR, L0_attn_b_KR, L0_attn_W_O, L0_attn_b_O) + _L0_ffn_ref(xn, L0_ffn_g_info, L0_ffn_W_qkv, L0_ffn_W_proj, L0_ffn_b_proj)
    return x

_drawn_inputs = setup_inputs


def setup_inputs(seed=0):
    import zlib

    import numpy as np

    out = dict(_drawn_inputs(seed))
    spreads = {'L0_ffn_b_proj': (0.0, 0.8)}
    factors = {'L0_attn_W_DQ': 8.0,
     'L0_attn_b_DQ': 8.0,
     'L0_attn_W_UQ': 8.0,
     'L0_attn_b_UQ': 8.0,
     'L0_attn_W_DKV': 8.0,
     'L0_attn_b_DKV': 5.479,
     'L0_attn_W_UK': 8.0,
     'L0_attn_b_UK': 64.0,
     'L0_attn_W_UV': 4.837,
     'L0_attn_W_QR': 8.0,
     'L0_attn_b_QR': 8.0,
     'L0_attn_W_KR': 8.0,
     'L0_attn_b_KR': 64.0,
     'L0_attn_b_O': 24.52,
     'L0_ffn_g_info': 8.0,
     'L0_ffn_W_qkv': 8.0,
     'L0_ffn_W_proj': 8.0,
     'L0_attn_b_UV': 8.0}
    for name, (base, spread) in spreads.items():
        noise = np.random.default_rng([zlib.crc32(name.encode()), seed]).standard_normal(out[name].shape)
        drawn = base * np.exp(spread * noise) if base else spread * noise
        out[name] = jnp.asarray(drawn.astype(out[name].dtype))
    for name, factor in factors.items():
        out[name] = (out[name] * factor).astype(out[name].dtype)
    return out
```

```python
import concourse.bass as bass
from concourse import mybir
from contextlib import ExitStack

F32 = mybir.dt.float32
BF16 = mybir.dt.bfloat16
ALU = mybir.AluOpType
ACT = mybir.ActivationFunctionType
AX = mybir.AxisListType

B, S, D = 8, 1024, 256
HA, CA, DK = 8, 32, 128
HB, DB, REG = 16, 16, 5
P = 128
NC = S // P
HALF = S // 2
KD = D // P
PIECES = 4
QA, QB_ = HA // 4, HB // 4
BIG = float(2.0 ** 60)
SCALE_A = float((DK + CA) ** -0.5)
SCALE_B = float(DB ** -0.5)
EPS = 1e-5

TERMS_A1 = [(0, 0), (0, 1), (1, 0)]
TERMS_A2 = [(1, 1), (0, 2), (2, 0)]
TERMS_B = [(0, 0), (0, 1), (0, 2), (1, 0), (1, 1), (2, 0)]
A1_ROWS = 96 + 3
A2_ROWS = 96 + 2
B_MAX_ROWS = 96 + 2
B_ROWS = 96 + 4

SPLITS = ([("cq", 0, hf) for hf in range(2)] + [("kb", 0, hf) for hf in range(2)]
          + [("kt", q, hf) for q in range(QA) for hf in range(2)]
          + [("qk", t, hf) for t in range(4) for hf in range(2)])
NSPLIT = len(SPLITS)
ROOT_OPS = 5
N_A_SPLITS = 8
HEAVY = [("lat", 0, 0), ("lat", 0, 1)] + SPLITS[2:8] + [("va", 0, 0), ("va", 1, 0)] + SPLITS[8:]


def maxima(kind, q):
    return [(kind, h, c, hf) for h in range(4 * q, 4 * q + 4) for c in range(NC) for hf in range(2)]


PREP = [[j] for j in HEAVY] + [[j] for j in maxima("ma", 0)]
_second = maxima("ma", 1)
PREP += [[j] for j in _second[:4]] + [[("fa", 0, 0)]] + [[j] for j in _second[4:]]
PREP = [j[0] for j in PREP]


def stage1_jobs():
    head = [("fa", 1, 0)] + [("vb", c, 0) for c in range(NC)]
    rest = []
    for q in range(QB_):
        m = maxima("mb", q)
        part = [("rs", q, 0), ("rs", q, 1)] + m[:4] + ([("fb", q - 1, 0)] if q else []) + m[4:40]
        part += [("rt", q, 0), ("rt", q, 1)] + m[40:48] + [("rv", q, 0)] + m[48:]
        rest += part
    return head, rest


STEPS_A, STEPS_B = QA * 2 * NC, QB_ * 2 * NC
STEPS = STEPS_A + STEPS_B


def spread(groups, jobs, first, last):
    n = last - first
    for i, j in enumerate(jobs):
        groups[first + i * n // len(jobs)].append(j)


def schedule(prep):
    g = [[] for _ in range(STEPS)]
    head, rest = stage1_jobs()
    spread(g, head, 0, 5)
    spread(g, rest, 5, STEPS_A)
    g[STEPS_A].append(("fb", QB_ - 1, 0))
    if prep:
        spread(g, PREP[:len(HEAVY)], STEPS_A + 1, STEPS_A + 20)
        spread(g, PREP[len(HEAVY):], STEPS_A + 20, STEPS)
    for c in range(NC // 2):
        g[STEPS_A + STEPS_B // 2 + 1 + PIECES + c].append(("pr", c, 0))
    tail = [("pr", c, 0) for c in range(NC // 2, NC)]
    return g, tail


def place(prep):
    g, tail = schedule(prep)
    flat = [j for s in g for j in s] + tail
    return {j: i for i, j in enumerate(flat)}, len(flat)


AT, JOBS = place(True)
AT_LAST, JOBS_LAST = place(False)
AT_PREP = {j: i for i, j in enumerate(PREP)}
JOBS_PREP = len(PREP)
MAXIMA_SETS = QA + QB_
EVACS = QA * 2 + QB_ * 2
GROUPS = 2 * STEPS
LOADS_A = 3 + 1 + 3 + 3 + 3
LOADS_B = 14
PRIMED = 1


def step_of(k):
    if k < STEPS_A:
        return "a", k // (2 * NC), k // NC % 2, k % NC
    k -= STEPS_A
    return "b", k // NC % QB_, k // (NC * QB_), k % NC


class Tally:

    def __init__(self, eng, sem):
        self.eng, self.sem, self.base, self.n = eng, sem, 0, 0

    def link(self, ins):
        self.n += 1
        ins.then_inc(self.sem, 1)

    def settle(self):
        self.eng.wait_ge(self.sem, self.base + self.n)


def build(nc, io, out):
    ctx = ExitStack()
    with ctx:
        program(nc, ctx, io, out)


def program(nc, ctx, io, out):
    def sb(name, shape, dt=F32):
        return ctx.enter_context(nc.sbuf_tensor(name, shape, dt))

    def pb(name, cols):
        return ctx.enter_context(nc.psum_tensor(name, [P, cols], F32))

    def sem(name):
        return ctx.enter_context(nc.semaphore(name))

    def dram(name, shape, dt):
        return nc.dram_tensor(name, shape, dt, kind="Internal").ap()

    xn_d = dram("xn_d", [B, KD, P, S], F32)
    cq_d = dram("cq_d", [3, CA, S], BF16)
    kb_d = dram("kb_d", [3, HA, S], BF16)
    kt_d = dram("kt_d", [3, HA * CA, S], BF16)
    qk_d = dram("qk_d", [2, 3, D, S], BF16)
    mask_d = dram("mask_d", [2, P, P], BF16)
    mask_rows = mask_d.rearrange("s (w b c) i -> s w b (c i)", w=2, b=B)

    KB = sb("KB", [P, HB, S], BF16)
    QB = sb("QB", [P, HB, S], BF16)
    KA1 = sb("KA1", [P, HA, S], BF16)
    KA2 = sb("KA2", [P, HA, S], BF16)
    QA1 = sb("QA1", [P, S], BF16)
    QA2 = sb("QA2", [P, HA, S], BF16)
    PT = sb("PT", [P, 2, 4, HALF])
    VB = sb("VB", [P, NC, HB, 32])
    VA = sb("VA", [P, NC, CA])
    xnT = sb("xnT", [P, KD, S])
    xb = sb("xb", [P, NC // 2, D])
    OA = sb("OA", [P, QA, S])
    OB = sb("OB", [P, QB_, HALF])
    rd = sb("rd", [P, HALF])
    shared = sb("shared", [P, 3 * S])
    latT = shared[:, 0:S]
    sp_ = shared[:, S:S + 1536].bitcast(BF16).rearrange("p (a t c) -> p a t c", a=2, t=3)
    r_ = shared[:, S + 1536:S + 1536 + HALF]
    SR = shared[:, 0:S]
    PRT = shared[:, S:2 * S].rearrange("p (c q) -> p c q", c=NC)
    Wqkv = sb("Wqkv", [P, KD, 3 * D])
    Wlat = sb("Wlat", [P, KD, 96])
    Wp = sb("Wp", [P, QB_, D])
    NA = sb("NA", [P, QA, D])
    Gk = sb("Gk", [97, HA, CA])
    Gb = sb("Gb", [97, HA])
    cst = sb("cst", [P, D])
    ident = sb("ident", [P, P])
    ones32 = sb("ones32", [P, 32])
    bdkv = sb("bdkv", [P, CA])
    blat = sb("blat", [96, 1])
    QR = sb("QR", [P, HB, 32], BF16)
    mx = sb("mx", [P, 2, 32, 2])
    nmx = sb("nmx", [P, 32])
    sh = sb("sh", [32, 2, P], BF16)
    rmx = sb("rmx", [P, 2])
    ORn = sb("ORn", [P, QB_, 8])
    rt1 = sb("rt1", [P, 8])
    simT = sb("simT", [P, B * NC])
    small = sb("small", [P, 64])
    tmp = QB[:, :, :].rearrange("p h s -> p (h s)").bitcast(F32)
    o = [0]

    def take(n):
        o[0] += n
        return tmp[:, o[0] - n:o[0]]

    Lp = take(HA * 97).rearrange("p (h c) -> p h c", h=HA)
    Rp = take(HA * 33).rearrange("p (h c) -> p h c", h=HA)
    KRp = take(HA * 33).rearrange("p (h c) -> p h c", h=HA)
    sel = take(97)
    Wuv = take(HA * CA).rearrange("p (h c) -> p h c", h=HA)
    Wo = take(HA * D).rearrange("p (h c) -> p h c", h=HA)
    buv = take(HA)
    buvb = take(HA * P).rearrange("p (h c) -> p h c", h=HA)
    bo = take(D)
    bp = take(D)
    g_bc = take(D)
    g_sq = take(D)
    wq_x = take(KD * (D + HB)).rearrange("p (k c) -> p k c", k=KD)
    masks = take(4 * 64).rearrange("p (s w c) -> p s w c", s=2, w=2)
    mask_bf = take(P).bitcast(BF16).rearrange("p (s c) -> p s c", s=2)
    tmp2 = KA1[:, :, :].rearrange("p h s -> p (h s)").bitcast(F32)
    NH = B * NC * HB
    n2, dots, root, newton = [tmp2[:, NH * i:NH * i + NH] for i in range(4)]
    xin = PT[:, 0, :, :].rearrange("p j c -> p (j c)").rearrange("p (f c d) -> p f c d", f=2, c=4)
    xn = PT[:, 1, :, :].rearrange("p j c -> p (j c)").rearrange("p (f c d) -> p f c d", f=2, c=4)
    sq = OB[:, :, :].rearrange("p q c -> p (q c)").rearrange("p (f c d) -> p f c d", f=2, c=4)

    stats = small[:, 0:24].rearrange("p (c s) -> p c s", c=4)
    mv = small[:, 24:32].rearrange("p (c s) -> p c s", c=4)
    rstd, var, tiny = small[:, 32:36], small[:, 36:40], small[:, 40:44]

    Sg = [pb(f"S{i}", 2 * HALF) for i in range(2)]
    O = [pb(f"O{i}", HALF) for i in range(2)]
    M = [pb(f"M{i}", HALF) for i in range(2)]

    passed = sem("passed")
    w_in = sem("w_in")
    const_ready = sem("const_ready")
    filled = sem("filled")
    setup_pe = sem("setup_pe")
    setup_dve = sem("setup_dve")
    x_in = [sem(f"x_in{f}") for f in range(2)]
    ln_done = [sem(f"ln_done{f}") for f in range(2)]
    t_done = [sem(f"t_done{f}") for f in range(2)]
    xt_ready = [sem(f"xt_ready{f}") for f in range(2)]
    xt_out = [sem(f"xt_out{f}") for f in range(2)]
    q_ready = [sem(f"q_ready{c}") for c in range(4)]
    q_used = [sem(f"q_used{c}") for c in range(4)]
    sim_done = [sem(f"sim_done{f}") for f in range(2)]
    root_in = sem("root_in")
    root_out = sem("root_out")
    ext_ready = sem("ext_ready")
    ext_all = sem("ext_all")
    mask_ready = sem("mask_ready")
    mask_t = sem("mask_t")
    mask_row = sem("mask_row")
    mask_out = sem("mask_out")
    chain = sem("chain")
    m_full = sem("m_full")
    m_free = sem("m_free")
    s_full = sem("s_full")
    e_done = sem("e_done")
    pv_done = sem("pv_done")
    ev_done = sem("ev_done")
    reg_fix = sem("reg_fix")
    nm_ready = sem("nm_ready")
    sh_in = sem("sh_in")
    cq_ready = sem("cq_ready")
    r_used = sem("r_used")
    st = [sem(f"st{i}") for i in range(2)]
    xn_in = sem("xn_in")
    ld_a = sem("ld_a")
    ld_b = [sem(f"ld_b{q}") for q in range(QB_)]
    qr_ready = sem("qr_ready")
    sr_ready = sem("sr_ready")
    pr_ready = sem("pr_ready")
    xb_in = sem("xb_in")
    xb_ready = sem("xb_ready")
    out_done = sem("out_done")

    N_W = 15 * 16

    def wait_apart(eng, what, count):
        eng.wait_ge(what, count)
        eng.sem_inc(passed, 1)

    def job_at(b, table, job):
        return JOBS_PREP + b * JOBS + table[job]

    def bank(i):
        return M[i % 2]

    def prime(eng, *sems):
        for one in sems:
            eng.sem_inc(one, PRIMED)

    w_loads = []

    def load_weights(sp):
        def ld(dst, src):
            w_loads.append(1)
            sp.dma_start(dst, src).then_inc(w_in, 16)
        ld(Wqkv[:, :, :], io["W_qkv"].rearrange("(k p) n -> p k n", p=P))
        ld(g_bc, io["g"].partition_broadcast(P))
        ld(Lp, io["L"])
        ld(Rp, io["R"])
        ld(KRp[0:CA], io["KR"])
        ld(sel[0:CA, :], io["sel"])
        ld(Wuv, io["WuvT"])
        ld(Wo, io["Wo"])
        ld(buv, io["buv"])
        ld(bo, io["bo"].partition_broadcast(P))
        ld(bp, io["bp"].partition_broadcast(P))
        ld(Wlat[:, :, :], io["Wlat"].rearrange("(k p) n -> p k n", p=P))
        ld(Wp[:, :, :], io["Wp"])
        ld(bdkv[:, :], io["bdkv"].partition_broadcast(P))
        ld(blat[:, :], io["blat"])

    block = ctx.enter_context(nc.Block())

    @block.sync
    def _(sp):
        prime(sp, out_done)
        load_weights(sp)
        with sp.Fori(0, B) as b:
            for f in range(2):
                wait_apart(sp, ln_done[f], PRIMED + b)
                sp.dma_start(xin[:, f], io["x"][b, f * HALF:(f + 1) * HALF, :].rearrange("(c p) d -> p c d", p=P)
                             ).then_inc(x_in[f], 16)
        wait_apart(sp, mask_row, 2)
        for s in range(2):
            sp.dma_start(mask_d[s], mask_bf[:, s, :]).then_inc(mask_out, 16)
        wait_apart(sp, mask_out, 32)

        def load_xn(n):
            sp.dma_start(xnT[:, :, :], xn_d[n].rearrange("k p s -> p k s")).then_inc(xn_in, 16)

        def store_splits(n, some):
            for i in some:
                kind, t, hf = SPLITS[i]
                cols = slice(hf * HALF, (hf + 1) * HALF)
                wait_apart(sp, r_used, n * (2 * NSPLIT) + (2 * i + 2))
                if kind == "cq":
                    dst, rows = cq_d[:, :, cols], CA
                elif kind == "kb":
                    dst, rows = kb_d[:, :, cols], HA
                elif kind == "kt":
                    dst, rows = kt_d[:, t * P:(t + 1) * P, cols], P
                else:
                    dst, rows = qk_d[t // 2, :, t % 2 * P:(t % 2 + 1) * P, cols], P
                sp.dma_start(dst.rearrange("t p c -> p t c"), sp_[0:rows, i % 2]).then_inc(st[i % 2], 16)

        def stores_done(n, k):
            for i in range(2):
                wait_apart(sp, st[i], n * (NSPLIT * 8) + k * 8)

        def load_a():
            for i, (kp, qp) in enumerate(TERMS_A1):
                rows = slice(CA * i, CA * i + CA)
                sp.dma_start(KA1[rows], kt_d[kp].rearrange("(h i) t -> i h t", i=CA)).then_inc(ld_a, 16)
                sp.dma_start(QA1[rows], cq_d[qp]).then_inc(ld_a, 16)
            sp.dma_start(KA1[96:99], kb_d).then_inc(ld_a, 16)
            for i, (kp, qp) in enumerate(TERMS_A2):
                rows = slice(CA * i, CA * i + CA)
                sp.dma_start(KA2[rows], kt_d[kp].rearrange("(h i) t -> i h t", i=CA)).then_inc(ld_a, 16)
                sp.dma_start(QA2[rows], cq_d[qp].unsqueeze(1).to_broadcast([CA, HA, S])).then_inc(ld_a, 16)

        def load_b(b):
            for q in range(QB_):
                hs = slice(4 * q, 4 * q + 4)
                for i, (kp, qp) in enumerate(TERMS_B):
                    rows = slice(DB * i, DB * i + DB)
                    for side, dst, part in ((1, KB, kp), (0, QB, qp)):
                        src = qk_d[side, part, 64 * q:64 * q + 64, :].rearrange("(h d) t -> d h t", d=DB)
                        sp.dma_start(dst[rows, hs], src).then_inc(ld_b[q], 16)
                for s, dst in ((0, KB), (1, QB)):
                    src = mask_rows[s, :, b, :].unsqueeze(1).to_broadcast([2, 4, S])
                    sp.dma_start(dst[96:98, hs], src).then_inc(ld_b[q], 16)

        def shift(job_index, dst, row, q):
            wait_apart(sp, m_free, job_index + 1)
            for w in range(2):
                sp.dma_start(dst[row + w:row + w + 1, 4 * q:4 * q + 4, :].rearrange("w h (c i) -> w (h c) i", i=P),
                             sh[:, w, :]).then_inc(sh_in, 16)

        def load_residual(b, f):
            sp.dma_start(xb[:, :, :], io["x"][b, f * HALF:(f + 1) * HALF, :].rearrange("(c p) d -> p c d", p=P)
                         ).then_inc(xb_in, 16)

        def store_out(b, f, table):
            wait_apart(sp, m_free, job_at(b, table, ("pr", 4 * f + 3, 0)) + 1)
            sp.dma_start(out[b, f * HALF:(f + 1) * HALF, :].rearrange("(c p) d -> p c d", p=P), xb[:, :, :]
                         ).then_inc(out_done, 16)

        for f in range(2):
            wait_apart(sp, xt_out[f], PRIMED + B * 16)
        load_xn(0)
        store_splits(0, range(N_A_SPLITS))
        stores_done(0, N_A_SPLITS)
        load_a()
        store_splits(0, range(N_A_SPLITS, NSPLIT))
        stores_done(0, NSPLIT)
        load_b(0)
        shift(AT_PREP[("fa", 0, 0)], QA2, 96, 0)

        def batch(b, prep, table):
            shift(job_at(b, table, ("fa", 1, 0)), QA2, 96, 1)
            wait_apart(sp, out_done, PRIMED + b * 32)
            load_residual(b, 0)
            if prep:
                wait_apart(sp, m_full, job_at(b, table, ("vb", NC - 1, 0)) + 1)
                load_xn(b + 1)
            for q in range(QB_):
                shift(job_at(b, table, ("fb", q, 0)), QB, 98, q)
            if prep:
                wait_apart(sp, ld_a, (b + 1) * (16 * LOADS_A))
                for q in range(QB_):
                    wait_apart(sp, ld_b[q], (b + 1) * (16 * LOADS_B))
                store_splits(b + 1, range(N_A_SPLITS))
                stores_done(b + 1, N_A_SPLITS)
                wait_apart(sp, pv_done, PRIMED + b * STEPS + STEPS_A)
                load_a()
                store_splits(b + 1, range(N_A_SPLITS, NSPLIT))
                shift(job_at(b, table, ("fa", 0, 0)), QA2, 96, 0)
            store_out(b, 0, table)
            wait_apart(sp, out_done, PRIMED + b * 32 + 16)
            load_residual(b, 1)
            if prep:
                stores_done(b + 1, NSPLIT)
                wait_apart(sp, pv_done, PRIMED + (b + 1) * STEPS)
                load_b(b + 1)
            store_out(b, 1, table)

        with sp.Fori(0, B - 1) as b:
            batch(b, True, AT)
        batch(B - 1, False, AT_LAST)
        wait_apart(sp, out_done, PRIMED + B * 32)

    @block.gpsimd
    def _(pool):
        fills = [(ident[:, :], 0.0), (ones32[:, :], 1.0), (VB[:, :, :, DB:32], 1.0),
                 (QA1[96:99, :], 1.0), (KA2[96:98, :, :], 1.0), (KB[96:100, :, :], 1.0),
                 (QR[96:98, :, :], 0.0), (QR[96:97, :, :], -BIG)]
        for i, (where, value) in enumerate(fills):
            nc.gpsimd.memset(where, value).then_inc(filled, 1)
            pool.wait_ge(filled, i + 1)
        nc.gpsimd.affine_select(out=ident[:, :], in_=ident[:, :], compare_op=ALU.not_equal, fill=1.0, base=0,
                                pattern=[[-1, P]], channel_multiplier=1).then_inc(const_ready, 1)
        pool.wait_ge(ext_ready, 1)
        nc.gpsimd.partition_all_reduce(small[:, 8:10], small[:, 0:2], P, bass.bass_isa.ReduceOp.max
                                       ).then_inc(ext_all, 1)

        def splits(n, at):
            for i, (kind, t, hf) in enumerate(SPLITS):
                rows = {"cq": CA, "kb": HA}.get(kind, P)
                part = sp_[0:rows, i % 2]
                if kind == "cq":
                    wait_apart(pool, cq_ready, n * 2 + (hf + 1))
                else:
                    wait_apart(pool, m_free, at((kind, t, hf)) + 1)
                nc.gpsimd.tensor_copy(part[:, 1, :], r_[0:rows, :]).then_inc(r_used, 1)
                pool.wait_ge(r_used, n * (2 * NSPLIT) + (2 * i + 1))
                nc.gpsimd.tensor_tensor(part[:, 2, :], r_[0:rows, :], part[:, 1, :], ALU.subtract
                                        ).then_inc(r_used, 1)

        def residual(b, f):
            pool.wait_ge(xb_in, b * 32 + (16 * f + 16))
            nc.gpsimd.tensor_tensor(xb[:, :, :], xb[:, :, :], cst[:, :].unsqueeze(1).to_broadcast([P, NC // 2, D]),
                                    ALU.add).then_inc(xb_ready, 1)

        splits(0, lambda j: AT_PREP[j])

        def batch(b, prep, table):
            for q in range(QB_):
                wait_apart(pool, m_full, JOBS_PREP + b * JOBS)
                wait_apart(pool, ld_b[q], (b + 1) * (16 * LOADS_B))
                nc.gpsimd.tensor_copy(QR[0:96, 4 * q:4 * q + 4, :], QB[0:96, 4 * q:4 * q + 4, 0:32]
                                      ).then_inc(qr_ready, 1)
            residual(b, 0)
            if prep:
                splits(b + 1, lambda j: job_at(b, table, j))
            residual(b, 1)

        with pool.Fori(0, B - 1) as b:
            batch(b, True, AT)
        batch(B - 1, False, AT_LAST)

    @block.scalar
    def _(act):
        prime(act, *xt_ready, *xt_out, *q_used)
        act.wait_ge(root_in, 1)
        nc.scalar.activation(small[:, 32:48], small[:, 16:32], ACT.Sqrt).then_inc(root_out, 1)
        with act.Fori(0, B) as b:
            for f in range(2):
                act.wait_ge(root_in, b * 2 + (f + 2))
                nc.scalar.activation(rstd, var, ACT.Sqrt).then_inc(root_out, 1)
            for f in range(2):
                act.wait_ge(t_done[f], PRIMED + b + 1)
                act.wait_ge(xt_out[f], PRIMED + b * 16)
                nc.scalar.activation(xnT[:, :, f * HALF:(f + 1) * HALF],
                                     Sg[f][:, :].rearrange("p (k s) -> p k s", k=KD), ACT.Copy
                                     ).then_inc(xt_ready[f], 1)
                act.wait_ge(xt_ready[f], PRIMED + b + 1)
                act.dma_start(xn_d[b, :, :, f * HALF:(f + 1) * HALF].rearrange("k p s -> p k s"),
                              xnT[:, :, f * HALF:(f + 1) * HALF]).then_inc(xt_out[f], 16)
                act.wait_ge(sim_done[f], PRIMED + b)
                for c in range(4):
                    act.wait_ge(q_ready[c], b * 2 + (f + 1))
                    nc.scalar.activation(sq[:, f, c, :], [M[0], M[1], O[0], O[1]][c][:, 0:D], ACT.Square)
                    nc.scalar.activation(dots[:, bass.ds(b * (NC * HB) + HB * (4 * f + c), HB)],
                                         [M[0], M[1], O[0], O[1]][c][:, D:D + HB], ACT.Copy).then_inc(q_used[c], 1)
        act.wait_ge(root_in, 2 * B + 2)
        nc.scalar.activation(root, n2, ACT.Sqrt).then_inc(root_out, 1)

        _, rest = stage1_jobs()
        groups, _ = schedule(True)
        reg_after = {}
        for k, jobs in enumerate(groups):
            for j in jobs:
                if j[0] == "rs" and j[2] == 1:
                    reg_after[k + 1] = j[1]

        def batch(b):
            for k in range(STEPS):
                kind = step_of(k)[0]
                if k > 1:
                    act.wait_ge(pv_done, PRIMED + b * STEPS + (k - 1))
                elif k == 0:
                    act.wait_ge(pv_done, PRIMED + b * STEPS)
                for pair in range(2):
                    act.wait_ge(s_full, b * GROUPS + (2 * k + pair + 1))
                    nc.scalar.activation(PT[:, k % 2, 2 * pair:2 * pair + 2, :],
                                         Sg[pair][:, :].rearrange("p (j s) -> p j s", j=2), ACT.Exp,
                                         scale=SCALE_A if kind == "a" else SCALE_B).then_inc(e_done, 1)
                if k in reg_after:
                    q = reg_after[k]
                    act.wait_ge(sr_ready, b * QB_ + (q + 1))
                    nc.scalar.activation(SR, SR, ACT.Exp, bias=rmx[:, 1:2], scale=SCALE_B).then_inc(pr_ready, 1)

        with act.Fori(0, B - 1) as b:
            batch(b)
        batch(B - 1)

    @block.tensor
    def _(pe):
        prime(pe, *t_done, pv_done)
        mm = nc.tensor.matmul
        pe.wait_ge(w_in, N_W)
        pe.wait_ge(const_ready, 1)
        for h in range(HA):
            g = Sg[0][0:97, 64 * h:64 * h + 33]
            mm(g, Lp[:, h, :], Rp[:, h, :], start=True, stop=False)
            last = mm(g, sel[0:CA, :], KRp[0:CA, h, :], start=False, stop=True)
        last.then_inc(setup_pe, 1)
        for h in range(HA):
            j, q = h % 4, h // 4
            last = mm(O[q][32 * j:32 * j + 32, 0:D], Wuv[:, h, :], Wo[:, h, :], start=True, stop=True)
        last.then_inc(setup_pe, 1)
        pe.wait_ge(setup_dve, 1)
        for h in range(HA):
            last = mm(M[0][:, 0:D], buvb[:, h, :], Wo[:, h, :], start=(h == 0), stop=(h == HA - 1))
        last.then_inc(setup_pe, 1)
        pe.wait_ge(setup_dve, 2)

        with pe.Fori(0, B) as b:
            for f in range(2):
                pe.wait_ge(ln_done[f], PRIMED + b + 1)
                pe.wait_ge(xt_ready[f], PRIMED + b)
                for k in range(KD):
                    for c in range(4):
                        last = nc.tensor.transpose(Sg[f][:, HALF * k + P * c:HALF * k + P * (c + 1)],
                                                   xn[:, f, c, P * k:P * (k + 1)], ident[:, :])
                last.then_inc(t_done[f], 1)
                pe.wait_ge(xt_ready[f], PRIMED + b + 1)
                for c in range(4):
                    pe.wait_ge(q_used[c], PRIMED + b * 2 + f)
                    for k in range(KD):
                        at = f * HALF + c * P
                        last = mm([M[0], M[1], O[0], O[1]][c][:, 0:D + HB], xnT[:, k, at:at + P],
                                  wq_x[:, k, :], start=(k == 0), stop=(k == KD - 1))
                    last.then_inc(q_ready[c], 1)
        pe.wait_ge(mask_ready, 1)
        for f in range(2):
            pe.wait_ge(q_used[f], PRIMED + 2 * B)
            nc.tensor.transpose(M[f][:, 0:P], masks[:, f, :, :].rearrange("p w c -> p (w c)"), ident[:, :]
                                ).then_inc(mask_t, 1)
        pe.wait_ge(mask_row, 2)

        def job(j, i, first, n, b, table):
            if not first:
                pe.wait_ge(m_free, i - 1)
            kind, x, y = j[0], j[1], j[2]
            m = bank(table[j] + JOBS_PREP * (b is not None))
            if kind == "va":
                for c in range(4):
                    for k in range(KD):
                        at = (4 * x + c) * P
                        last = mm(m[:, CA * c:CA * c + CA], xnT[:, k, at:at + P], Wlat[:, k, CA:2 * CA],
                                  start=(k == 0), stop=(k == KD - 1))
            elif kind == "vb":
                for k in range(KD):
                    last = mm(m[:, 0:D], xnT[:, k, x * P:(x + 1) * P], Wqkv[:, k, 2 * D:3 * D],
                              start=(k == 0), stop=(k == KD - 1))
            elif kind == "lat":
                if y == 0:
                    pe.wait_ge(xn_in, n * 16 + 16)
                for k in range(KD):
                    last = mm(m[0:96, :], Wlat[:, k, :], xnT[:, k, y * HALF:(y + 1) * HALF],
                              start=(k == 0), stop=(k == KD - 1))
            elif kind in ("kb", "kt"):
                if kind == "kb" and y == 0:
                    at = AT_PREP[("lat", 0, 1)] if b is None else job_at(b, table, ("lat", 0, 1))
                    pe.wait_ge(m_free, at + 1)
                lhs = Gb[:, :] if kind == "kb" else Gk[:, 4 * x:4 * x + 4, :].rearrange("p h i -> p (h i)")
                rows = HA if kind == "kb" else P
                last = mm(m[0:rows, :], lhs, latT[0:97, y * HALF:(y + 1) * HALF], start=True, stop=True)
            elif kind == "qk":
                for k in range(KD):
                    last = mm(m[:, :], Wqkv[:, k, P * x:P * x + P], xnT[:, k, y * HALF:(y + 1) * HALF],
                              start=(k == 0), stop=(k == KD - 1))
            elif kind == "ma":
                h, c, hf = j[1:]
                if h == 0 and c == 0 and hf == 0:
                    pe.wait_ge(ld_a, n * (16 * LOADS_A) + 16 * LOADS_A)
                last = mm(m[:, :], QA1[0:A1_ROWS, c * P:(c + 1) * P], KA1[0:A1_ROWS, h, hf * HALF:(hf + 1) * HALF],
                          start=True, stop=True)
            elif kind == "mb":
                h, c, hf = j[1:]
                last = mm(m[:, :], QB[0:B_MAX_ROWS, h, c * P:(c + 1) * P],
                          KB[0:B_MAX_ROWS, h, hf * HALF:(hf + 1) * HALF], start=True, stop=True)
            elif kind in ("fa", "fb"):
                if b is None:
                    pe.wait_ge(nm_ready, 1)
                else:
                    s = {("fa", 1): 2, ("fa", 0): QB_ + 3}.get((kind, x), x + 3)
                    pe.wait_ge(nm_ready, b * MAXIMA_SETS + s)
                last = nc.tensor.transpose(m[0:32, 0:P], nmx[:, :], ident[:, :])
            elif kind == "rs":
                if y == 0:
                    pe.wait_ge(ld_b[x], n * (16 * LOADS_B) + 16 * LOADS_B)
                    pe.wait_ge(qr_ready, b * QB_ + (x + 1))
                for jj in range(4):
                    last = mm(m[32 * jj:32 * jj + 32, :], QR[0:B_MAX_ROWS, 4 * x + jj, :],
                              KB[0:B_MAX_ROWS, 4 * x + jj, y * HALF:(y + 1) * HALF], start=True, stop=True)
            elif kind == "rt":
                if y == 0:
                    pe.wait_ge(pr_ready, b * QB_ + (x + 1))
                for c in range(4):
                    at = (4 * y + c) * P
                    last = nc.tensor.transpose(m[:, c * P:(c + 1) * P], SR[:, at:at + P], ident[:, :])
            elif kind == "rv":
                pe.wait_ge(m_free, job_at(b, table, ("rt", x, 1)) + 1)
                for c in range(NC):
                    for jj in range(4):
                        last = mm(m[32 * jj:32 * jj + 32, 0:8], VB[:, c, 4 * x + jj, :],
                                  PRT[:, c, 32 * jj:32 * jj + 8], start=(c == 0), stop=(c == NC - 1),
                                  skip_group_check=True)
            elif kind == "pr":
                if x == 0:
                    pe.wait_ge(ev_done, PRIMED + b * EVACS + (2 * QA + QB_))
                    pe.wait_ge(reg_fix, (b + 1) * QB_)
                if x == NC // 2:
                    pe.wait_ge(ev_done, PRIMED + (b + 1) * EVACS)
                for q in range(QA):
                    mm(m[:, 0:D], OA[:, q, x * P:(x + 1) * P], NA[:, q, :], start=(q == 0), stop=False)
                at = (x % 4) * P
                for q in range(QB_):
                    last = mm(m[:, 0:D], OB[:, q, at:at + P], Wp[:, q, :], start=False, stop=(q == QB_ - 1))
            last.then_inc(m_full, 1)

        def scores(b, k, jj):
            kind, q, hf, c = step_of(k)
            if kind == "a" and hf == 0 and c == 0 and jj == 0:
                pe.wait_ge(sh_in, b * (32 * MAXIMA_SETS) + 32 * (q + 1))
            if kind == "b" and hf == 0 and c == 0 and jj == 0:
                pe.wait_ge(sh_in, b * (32 * MAXIMA_SETS) + 32 * (q + 3))
            qs, ks = slice(hf * HALF, (hf + 1) * HALF), slice(c * P, (c + 1) * P)
            pair = jj // 2
            if k and jj % 2 == 0:
                pe.wait_ge(e_done, b * GROUPS + (2 * k + pair - 1))
            h = 4 * q + jj
            to = Sg[pair][:, jj % 2 * HALF:(jj % 2 + 1) * HALF]
            if kind == "a":
                mm(to, KA1[0:A1_ROWS, h, ks], QA1[0:A1_ROWS, qs], start=True, stop=False)
                last = mm(to, KA2[0:A2_ROWS, h, ks], QA2[0:A2_ROWS, h, qs], start=False, stop=True)
            else:
                last = mm(to, KB[0:B_ROWS, h, ks], QB[0:B_ROWS, h, qs], start=True, stop=True)
            if jj % 2:
                last.then_inc(s_full, 1)

        def values(b, k):
            kind, q, hf, c = step_of(k)
            if c == 0:
                if kind == "a":
                    pe.wait_ge(ev_done, PRIMED + b * EVACS + (2 * q + hf))
                else:
                    pe.wait_ge(ev_done, PRIMED + b * EVACS + (2 * QA + max(0, hf * QB_ + q - 1)))
            pe.wait_ge(e_done, b * GROUPS + (2 * k + 2))
            o = O[0] if kind == "a" else O[q % 2]
            for jj in range(4):
                lhs = VA[:, c, :] if kind == "a" else VB[:, c, 4 * q + jj, :]
                last = mm(o[32 * jj:32 * jj + 32, :], lhs, PT[:, k % 2, jj, :], start=(c == 0), stop=(c == NC - 1),
                          skip_group_check=True)
            if kind == "b":
                last.then_inc(pv_done, 1)

        def denominators(b, k):
            kind, q, hf, c = step_of(k)
            for jj in range(4):
                last = mm(O[1][32 * jj:32 * jj + 32, :], ones32[:, :], PT[:, k % 2, jj, :],
                          start=(c == 0), stop=(c == NC - 1), skip_group_check=True)
            last.then_inc(pv_done, 1)

        for i, j in enumerate(PREP):
            job(j, i, i < 2, 0, None, AT_PREP)

        def batch(b, prep, table):
            groups, tail = schedule(prep)

            def some_jobs(k, part):
                todo = groups[k]
                for j in todo[part * len(todo) // 6:(part + 1) * len(todo) // 6]:
                    n = b + 1 if j[0] in ("va", "lat", "kb", "kt", "qk", "ma") else b
                    job(j, job_at(b, table, j), False, n, b, table)

            for k in range(STEPS):
                for jj in range(4):
                    scores(b, k, jj)
                    some_jobs(k, jj)
                if k:
                    values(b, k - 1)
                some_jobs(k, 4)
                if k and step_of(k - 1)[0] == "a":
                    denominators(b, k - 1)
                some_jobs(k, 5)
            values(b, STEPS - 1)
            for j in tail:
                job(j, job_at(b, table, j), False, b, b, table)

        with pe.Fori(0, B - 1) as b:
            batch(b, True, AT)
        batch(B - 1, False, AT_LAST)

    @block.vector
    def _(dve):
        v = nc.vector
        own = Tally(dve, chain)
        prime(dve, *ln_done, *sim_done, ev_done)

        def inverse(y, x, t):
            for link in (lambda: v.reciprocal(y, y),
                         lambda: v.tensor_tensor(t, y, y, ALU.mult),
                         lambda: v.tensor_tensor(t, t, x, ALU.mult),
                         lambda: v.tensor_scalar(t, t, -0.5, 1.5, ALU.mult, ALU.add),
                         lambda: v.tensor_tensor(y, y, t, ALU.mult)):
                own.link(link())
                own.settle()

        dve.wait_ge(w_in, N_W)
        own.link(v.tensor_copy(buvb, buv.unsqueeze(2).to_broadcast([P, HA, P])))
        own.settle()
        own.link(v.tensor_tensor(g_sq, g_bc, g_bc, ALU.mult))
        own.settle()
        v.tensor_reduce(small[:, 16:32], g_sq.rearrange("p (h d) -> p h d", d=DB), AX.X, ALU.add).then_inc(root_in, 1)
        dve.wait_ge(root_out, 1)
        inverse(small[:, 32:48], small[:, 16:32], small[:, 48:64])
        own.link(v.tensor_scalar(small[:, 32:48], small[:, 32:48], 1.0 / HB, None, ALU.mult))
        own.settle()
        own.link(v.tensor_tensor(g_sq.rearrange("p (h d) -> p h d", d=DB), g_bc.rearrange("p (h d) -> p h d", d=DB),
                                 small[:, 32:48].unsqueeze(2).to_broadcast([P, HB, DB]), ALU.mult))
        own.settle()
        for k in range(KD):
            own.link(v.tensor_copy(wq_x[:, k, 0:D], Wqkv[:, k, 0:D]))
            own.link(v.tensor_tensor(g_bc, Wqkv[:, k, 0:D], g_sq, ALU.mult))
            own.settle()
            own.link(v.tensor_reduce(wq_x[:, k, D:D + HB], g_bc.rearrange("p (h d) -> p h d", d=DB), AX.X, ALU.add))
            own.settle()
        v.tensor_tensor(bo, bo, bp, ALU.add).then_inc(setup_dve, 1)
        dve.wait_ge(setup_pe, 1)
        g = Sg[0][0:97, 0:HALF].rearrange("p (h c) -> p h c", h=HA)
        own.link(v.tensor_copy(Gk[:, :, :], g[:, :, 0:CA]))
        own.link(v.tensor_copy(Gb[:, :].unsqueeze(2), g[:, :, CA:CA + 1]))
        dve.wait_ge(setup_pe, 2)
        for q in range(QA):
            own.link(v.tensor_copy(NA[:, q, :], O[q][:, 0:D]))
        dve.wait_ge(setup_pe, 3)
        dve.wait_ge(setup_dve, 1)
        v.tensor_tensor(cst[:, :], M[0][:, 0:D], bo, ALU.add).then_inc(setup_dve, 1)

        n0, per = own.n, 2 * (4 + 4 + ROOT_OPS)
        with dve.Fori(0, B) as b:
            own.base, own.n = b * per + n0, 0
            for f in range(2):
                dve.wait_ge(x_in[f], b * 16 + 16)
                for c in range(4):
                    own.link(v.bn_stats(stats[:, c, :], xin[:, f, c, :]))
                wait_apart(dve, own.sem, own.base + own.n)
                for c in range(4):
                    own.link(v.bn_aggr(mv[:, c, :], stats[:, c, :]))
                own.settle()
                v.tensor_scalar(var, mv[:, :, 1], EPS, None, ALU.add).then_inc(root_in, 1)
                dve.wait_ge(root_out, b * 2 + (f + 2))
                inverse(rstd, var, tiny)
                dve.wait_ge(t_done[f], PRIMED + b)
                for c in range(4):
                    last = v.tensor_scalar(xn[:, f, c, :], xin[:, f, c, :], mv[:, c, 0:1], rstd[:, c:c + 1],
                                           ALU.subtract, ALU.mult)
                last.then_inc(ln_done[f], 1)
            for f in range(2):
                dve.wait_ge(q_used[3], PRIMED + b * 2 + (f + 1))
                v.tensor_reduce(n2[:, bass.ds(b * (NC * HB) + 64 * f, 64)],
                                sq[:, f].rearrange("p c (h d) -> p (c h) d", d=DB), AX.X, ALU.add
                                ).then_inc(sim_done[f], 1)
            assert own.n == per
        own.base, own.n = 0, n0 + B * per
        for f in range(2):
            dve.wait_ge(sim_done[f], PRIMED + B)
        own.link(v.memset(tiny[:, 0:1], 0.0))
        own.settle()
        v.tensor_copy(tiny[:, 1:2], tiny[:, 0:1]).then_inc(root_in, 1)
        dve.wait_ge(root_out, 2 * B + 2)
        inverse(root, n2, newton)
        for c in range(4):
            dve.wait_ge(q_used[c], PRIMED + 2 * B)
        own.link(v.tensor_tensor(root, root, dots, ALU.mult))
        own.settle()
        own.link(v.tensor_reduce(simT[:, :], root.rearrange("p (c h) -> p c h", h=HB), AX.X, ALU.add))
        own.settle()
        sv = simT[:, :].rearrange("p (b c) -> p b c", b=B)
        own.link(v.tensor_copy(sv[0:REG, :, 0], sv[0:REG, :, 1]))
        own.settle()
        own.link(v.tensor_reduce(small[:, 0:1], simT[:, :], AX.X, ALU.max))
        v.tensor_reduce(small[:, 1:2], simT[:, :], AX.X, ALU.min, negate=True).then_inc(ext_ready, 1)
        dve.wait_ge(ext_all, 1)
        own.link(v.tensor_scalar(small[:, 10:11], small[:, 9:10], -1.0, None, ALU.mult))
        own.link(v.tensor_tensor(small[:, 11:12], small[:, 8:9], small[:, 9:10], ALU.add))
        own.settle()
        own.link(v.reciprocal(small[:, 12:13], small[:, 11:12]))
        own.settle()
        own.link(v.tensor_scalar(simT[:, :], simT[:, :], small[:, 10:11], small[:, 12:13], ALU.subtract, ALU.mult))
        own.settle()
        own.link(v.tensor_scalar(masks[:, 0, 0, :], simT[:, :], 0.9, None, ALU.is_gt))
        own.settle()
        pos = masks[:, 0, 0, :]
        own.link(v.tensor_scalar(masks[:, 0, 1, :], pos, -1.0, 1.0, ALU.mult, ALU.add))
        own.link(v.tensor_scalar(masks[:, 1, 0, :], pos, BIG, -BIG, ALU.mult, ALU.add))
        own.link(v.tensor_scalar(masks[:, 1, 1, :], pos, -BIG, None, ALU.mult))
        own.settle()
        for s, w, val in ((0, 0, 0.0), (0, 1, 0.0), (1, 0, 0.0), (1, 1, -BIG)):
            own.link(v.memset(masks[0:REG, s, w, :].rearrange("p (b c) -> p b c", b=B)[:, :, 0], val))
        own.settle()
        v.tensor_copy(small[0:1, 60:61], small[0:1, 11:12]).then_inc(mask_ready, 1)
        for f in range(2):
            dve.wait_ge(mask_t, f + 1)
            v.tensor_copy(mask_bf[:, f, :], M[f][:, 0:P]).then_inc(mask_row, 1)

        def split(n, i, src, rows, done):
            if i >= 2:
                dve.wait_ge(st[i % 2], n * (NSPLIT * 8) + (i // 2) * 16)
            elif not (isinstance(n, int) and n == 0):
                dve.wait_ge(st[i % 2], n * (NSPLIT * 8))
            own.link(v.tensor_copy(sp_[0:rows, i % 2, 0, :], src))
            own.settle()
            if i or not isinstance(n, int):
                dve.wait_ge(r_used, n * (2 * NSPLIT) + 2 * i)
            v.tensor_tensor(r_[0:rows, :], src, sp_[0:rows, i % 2, 0, :], ALU.subtract).then_inc(done, 1)

        def combine(s):
            own.link(v.tensor_reduce(nmx[:, :], mx[:, s % 2], AX.X, ALU.max, negate=True))
            own.settle()
            v.tensor_copy(small[0:1, 61:62], nmx[0:1, 0:1]).then_inc(nm_ready, 1)

        def job(j, i, n, b, table):
            kind, x, y = j[0], j[1], j[2]
            if kind == "rv":
                wait_apart(dve, m_full, i + 1)
            else:
                dve.wait_ge(m_full, i + 1)
            m = bank(table[j] + JOBS_PREP * (b is not None))
            if kind == "va":
                v.tensor_tensor(VA[:, 4 * x:4 * x + 4, :], m[:, 0:P].rearrange("p (c i) -> p c i", c=4),
                                bdkv[:, :].unsqueeze(1).to_broadcast([P, 4, CA]), ALU.add).then_inc(m_free, 1)
            elif kind == "vb":
                if x == 0:
                    dve.wait_ge(pv_done, PRIMED + b * STEPS)
                v.tensor_copy(VB[:, x, :, 0:DB], m[:, 0:D].rearrange("p (h d) -> p h d", h=HB)).then_inc(m_free, 1)
            elif kind == "lat":
                cols = slice(y * HALF, (y + 1) * HALF)
                own.link(v.memset(latT[96:97, cols], 1.0))
                v.tensor_scalar(latT[0:96, cols], m[0:96, :], blat[:, 0:1], None, ALU.add).then_inc(m_free, 1)
                dve.wait_ge(m_free, i + 1)
                split(n, y, latT[0:CA, cols], CA, cq_ready)
            elif kind in ("kb", "kt", "qk"):
                rows = HA if kind == "kb" else P
                split(n, SPLITS.index(j), m[0:rows, :], rows, m_free)
            elif kind in ("ma", "mb"):
                h, c, hf = j[1:]
                s = h // 4 + (QA if kind == "mb" else 0)
                v.tensor_reduce(mx[:, s % 2, NC * (h % 4) + c, hf:hf + 1], m[:, :], AX.X, ALU.max).then_inc(m_free, 1)
                if h % 4 == 3 and c == NC - 1 and hf == 1:
                    dve.wait_ge(m_free, i + 1)
                    combine(s)
            elif kind in ("fa", "fb"):
                if b is None:
                    pass
                else:
                    s = {("fa", 1): 1, ("fa", 0): QB_ + 2}.get((kind, x), x + 2)
                    dve.wait_ge(sh_in, b * (32 * MAXIMA_SETS) + 32 * s)
                own.link(v.tensor_copy(sh[:, 0, :], m[0:32, 0:P]))
                own.settle()
                v.tensor_tensor(sh[:, 1, :], m[0:32, 0:P], sh[:, 0, :], ALU.subtract).then_inc(m_free, 1)
            elif kind == "rs":
                if x == 0 and y == 0:
                    for a in range(2):
                        dve.wait_ge(st[a], n * (NSPLIT * 8) + NSPLIT * 8)
                    dve.wait_ge(r_used, n * (2 * NSPLIT) + 2 * NSPLIT)
                v.tensor_copy(SR[:, y * HALF:(y + 1) * HALF], m[:, :]).then_inc(m_free, 1)
                if y == 1:
                    dve.wait_ge(m_free, i + 1)
                    own.link(v.tensor_reduce(rmx[:, 0:1], SR, AX.X, ALU.max))
                    own.settle()
                    v.tensor_scalar(rmx[:, 1:2], rmx[:, 0:1], -SCALE_B, None, ALU.mult).then_inc(sr_ready, 1)
            elif kind == "rt":
                v.tensor_copy(PRT[:, 4 * y:4 * y + 4, :], m[:, :].rearrange("p (c q) -> p c q", c=4)
                              ).then_inc(m_free, 1)
            elif kind == "rv":
                own.link(v.stream_shuffle(rt1[:, :], m[:, 0:8], [DB + a % DB for a in range(32)]))
                own.settle()
                own.link(v.reciprocal(rt1[:, :], rt1[:, :]))
                own.settle()
                v.scalar_tensor_tensor(ORn[:, x, :], m[:, 0:8], 0.5, rt1[:, :], ALU.mult, ALU.mult
                                       ).then_inc(m_free, 1)
            elif kind == "pr":
                if x % 4 == 0:
                    dve.wait_ge(xb_ready, b * 2 + (x // 4 + 1))
                v.tensor_tensor(xb[:, x % 4, :], m[:, 0:D], xb[:, x % 4, :], ALU.add).then_inc(m_free, 1)

        def normalise(b, k, pieces):
            kind, q, hf, c = step_of(k)
            before = 2 * q + hf if kind == "a" else 2 * QA + hf * QB_ + q
            if 0 in pieces:
                dve.wait_ge(ev_done, PRIMED + b * EVACS + before)
                wait_apart(dve, pv_done, PRIMED + b * STEPS + (k + 1))
            if kind == "a":
                own.link(v.reciprocal(rd[:, :], O[1][:, :]))
                own.settle()
                v.tensor_tensor(OA[:, q, hf * HALF:(hf + 1) * HALF], O[0][:, :], rd[:, :], ALU.mult
                                ).then_inc(ev_done, 1)
                return
            o = O[q % 2]
            for piece in pieces:
                cols = slice(piece * HALF // PIECES, (piece + 1) * HALF // PIECES)
                own.link(v.stream_shuffle(rd[:, cols], o[:, cols], [DB + a % DB for a in range(32)]))
                own.settle()
                own.link(v.reciprocal(rd[:, cols], rd[:, cols]))
                own.settle()
                last = v.tensor_tensor(OB[:, q, cols], o[:, cols], rd[:, cols], ALU.mult)
                if piece == PIECES - 1:
                    last.then_inc(ev_done, 1)
            if hf == 0 and PIECES - 1 in pieces:
                dve.wait_ge(ev_done, PRIMED + b * EVACS + (2 * QA + q + 1))
                v.scalar_tensor_tensor(OB[:, q, 0:REG], OB[:, q, 0:REG], 0.5, ORn[:, q, 0:REG], ALU.mult, ALU.add
                                       ).then_inc(reg_fix, 1)

        for i, j in enumerate(PREP):
            job(j, i, 0, None, AT_PREP)

        def batch(b, prep, table):
            groups, tail = schedule(prep)
            for k in range(STEPS):
                for j in groups[k]:
                    n = b + 1 if j[0] in ("va", "lat", "kb", "kt", "qk", "ma") else b
                    job(j, job_at(b, table, j), n, b, table)
                if k and step_of(k - 1)[0] == "a" and step_of(k - 1)[3] == NC - 1:
                    normalise(b, k - 1, [0])
                for piece in range(PIECES):
                    if k > STEPS_A + piece and step_of(k - 1 - piece)[3] == NC - 1:
                        normalise(b, k - 1 - piece, [piece])
            normalise(b, STEPS - 1, range(PIECES))
            for j in tail:
                job(j, job_at(b, table, j), b, b, table)

        n0 = own.n
        per = 2 + NSPLIT + MAXIMA_SETS + MAXIMA_SETS + 3 * QB_ + 2 * QA + 2 * QB_ * 2 * PIECES
        with dve.Fori(0, B - 1) as b:
            own.base, own.n = b * per + n0, 0
            batch(b, True, AT)
            assert own.n == per, (own.n, per)
        own.base, own.n = (B - 1) * per + n0, 0
        batch(B - 1, False, AT_LAST)


def kernel(**inputs):
    import numpy as np
    import concourse.bacc as bacc
    from concourse.bass_utils import run_bass_kernel_spmd

    a = {k: np.ascontiguousarray(v) for k, v in inputs.items()}
    at = {k[len("L0_attn_"):]: v for k, v in a.items() if k.startswith("L0_attn_")}
    ff = {k[len("L0_ffn_"):]: v for k, v in a.items() if k.startswith("L0_ffn_")}
    f32 = np.float32
    L = np.zeros((DK, HA, 97), f32)
    L[:, :, 32:64] = at["W_UK"].reshape(CA, HA, DK).transpose(2, 1, 0)
    L[:, :, 96] = at["b_UK"].reshape(HA, DK).T
    R = np.zeros((DK, HA, 33), f32)
    R[:, :, 0:32] = at["W_UQ"].reshape(CA, HA, DK).transpose(2, 1, 0)
    R[:, :, 32] = at["b_UQ"].reshape(HA, DK).T
    KR = np.zeros((CA, HA, 33), f32)
    KR[:, :, 0:32] = at["W_QR"].reshape(CA, HA, CA).transpose(2, 1, 0)
    KR[:, :, 32] = at["b_QR"].reshape(HA, CA).T
    sel = np.zeros((CA, 97), f32)
    sel[:, 64:96] = np.eye(CA, dtype=f32)
    Wp = np.zeros((4, 32, QB_, D), f32)
    Wp[:, 0:DB] = ff["W_proj"].reshape(QB_, 4, DB, D).transpose(1, 2, 0, 3)
    arrays = {
        "x": at["h_t"],
        "W_qkv": ff["W_qkv"],
        "g": ff["g_info"][0, 0],
        "L": L, "R": R, "KR": KR, "sel": sel,
        "WuvT": np.ascontiguousarray(at["W_UV"].reshape(CA, HA, DK).transpose(2, 1, 0)),
        "Wo": np.ascontiguousarray(at["W_O"].reshape(HA, DK, D).transpose(1, 0, 2)),
        "buv": np.ascontiguousarray(at["b_UV"].reshape(HA, DK).T),
        "bo": at["b_O"], "bp": ff["b_proj"],
        "Wlat": np.concatenate([at["W_DQ"], at["W_DKV"], at["W_KR"]], axis=1),
        "Wp": Wp.reshape(P, QB_, D),
        "bdkv": at["b_DKV"],
        "blat": np.concatenate([at["b_DQ"], at["b_DKV"], at["b_KR"]])[:, None],
    }
    arrays = {k: np.ascontiguousarray(v) for k, v in arrays.items()}
    nc = bacc.Bacc("TRN2", target_bir_lowering=False, num_devices=1)
    io = {k: nc.dram_tensor(f"in_{k}", v.shape, mybir.dt.from_np(v.dtype), kind="ExternalInput").ap()
          for k, v in arrays.items()}
    out = nc.dram_tensor("out_0", (B, S, D), F32, kind="ExternalOutput").ap()
    build(nc, io, out)
    r = run_bass_kernel_spmd(nc, [{f"in_{k}": v for k, v in arrays.items()}], core_ids=[0])
    return r.results[0]["out_0"]
```
